# Optimizing a Trainium2 kernel written in Bass

```python
import numpy as np
import jax
import jax.numpy as jnp

def _softmax(x, axis=-1):
    return jax.nn.softmax(x, axis=axis)

def _gelu(x):
    return jax.nn.gelu(x, approximate=True)

def _silu(x):
    return jax.nn.silu(x)

def _sigmoid(x):
    return jax.nn.sigmoid(x)

def _layernorm(x, axis=-1, eps=1e-05):
    m = jnp.mean(x, axis=axis, keepdims=True)
    v = jnp.var(x, axis=axis, keepdims=True)
    return (x - m) / jnp.sqrt(v + eps)

def _scatter_add(tgt, idx, src, axis=0):
    return tgt.at[idx].add(src)

def _segment_sum(src, seg, n):
    return jax.ops.segment_sum(src, seg, n)
kernel_name = 'mk_gnn_preln_d4_gnn_r32_f1f3e2'

def setup_inputs(seed: int=0):
    np.random.seed(seed)
    _w = jnp.asarray

    def _rec_inputs():
        import jax
        import jax.numpy as jnp
        _gk = jax.random.key(seed)
        x = -0.0002117 + 1 * jax.random.normal(jax.random.fold_in(_gk, 1), (10000, 512), jnp.float32)
        src = jax.random.randint(jax.random.fold_in(_gk, 2), (10000,), 0, 10000, jnp.int32)
        dst = jnp.minimum((10000 * jax.random.uniform(jax.random.fold_in(_gk, 3), (10000,)) ** 2.0).astype(jnp.int32), 9999)
        _o = jnp.argsort(dst, stable=True)
        src = src[_o]
        dst = dst[_o]
        edge_attr_512 = -8.513e-05 + 0.999844 * jax.random.normal(jax.random.fold_in(_gk, 13), (10000, 512), jnp.float32)
        return (x, src, dst, edge_attr_512)
    x, src, dst, edge_attr_512 = _rec_inputs()

    def _L0_gnn_setup():
        import jax, jax.numpy as jnp
        import numpy as np
        N_NODES = 50000
        N_EDGES = 12500
        IN_DIM = 512
        OUT_DIM = 512
        key = jax.random.key(seed)
        k1, k2, k3, k4 = jax.random.split(key, 4)
        x = jax.random.normal(k1, (N_NODES, IN_DIM), dtype=jnp.float32)
        edge_index = jax.random.randint(k2, (2, N_EDGES), 0, N_NODES, dtype=jnp.int64)
        W = jax.random.normal(k3, (OUT_DIM, IN_DIM), dtype=jnp.float32) / np.sqrt(IN_DIM)
        b = jax.random.normal(k4, (OUT_DIM,), dtype=jnp.float32) * 0.01
        return {'x': x, 'edge_index': edge_index, 'W': W, 'b': b}
    _L0_gnn_all = _L0_gnn_setup()
    _L0_gnn_in = {k: v for k, v in _L0_gnn_all.items() if k in ('W', 'b')}
    del _L0_gnn_all

    def _L1_gnn_setup():
        import jax, jax.numpy as jnp
        import numpy as np
        N = 10000
        E = 5000
        D = 512
        key = jax.random.key(seed)
        k1, k2, k3, k4, k5 = jax.random.split(key, 5)
        node_tokens = jax.random.normal(k1, (N, D), dtype=jnp.float32)
        relation_tokens = jax.random.normal(k2, (E, D), dtype=jnp.float32)
        edge_index = jax.random.randint(k3, (2, E), 0, N, dtype=jnp.int64)
        lim_m = float(np.sqrt(6.0 / (D + D)))
        Wm = jax.random.uniform(k4, (D, D), minval=-lim_m, maxval=lim_m, dtype=jnp.float32)
        bm = jnp.zeros((D,), dtype=jnp.float32)
        lim_u = float(np.sqrt(6.0 / (2 * D + D)))
        Wu = jax.random.uniform(k5, (D, 2 * D), minval=-lim_u, maxval=lim_u, dtype=jnp.float32)
        bu = jnp.zeros((D,), dtype=jnp.float32)
        gamma = jnp.ones((D,), dtype=jnp.float32)
        beta = jnp.zeros((D,), dtype=jnp.float32)
        return {'node_tokens': node_tokens, 'relation_tokens': relation_tokens, 'edge_index': edge_index, 'num_nodes': N, 'Wm': Wm, 'bm': bm, 'Wu': Wu, 'bu': bu, 'gamma': gamma, 'beta': beta}
    _L1_gnn_all = _L1_gnn_setup()
    _L1_gnn_in = {k: v for k, v in _L1_gnn_all.items() if k in ('Wm', 'bm', 'Wu', 'bu', 'gamma', 'beta')}
    del _L1_gnn_all

    def _L2_gnn_setup():
        import jax, jax.numpy as jnp
        import numpy as np
        N_NODES = 10000
        key = jax.random.key(seed)
        k1, k2, k3, k4, k5 = jax.random.split(key, 5)
        x = jax.random.normal(k1, (N_NODES, 512), dtype=jnp.float32)
        edge_index = jax.random.randint(k2, (2, 5000), 0, N_NODES, dtype=jnp.int64)
        W_l = jax.random.normal(k3, (512, 512), dtype=jnp.float32) * 0.04
        b_l = jax.random.normal(k4, (512,), dtype=jnp.float32) * 0.04
        W_r = jax.random.normal(k5, (512, 512), dtype=jnp.float32) * 0.04
        return {'x': x, 'edge_index': edge_index, 'W_l': W_l, 'b_l': b_l, 'W_r': W_r}
    _L2_gnn_all = _L2_gnn_setup()
    _L2_gnn_in = {k: v for k, v in _L2_gnn_all.items() if k in ('W_l', 'b_l', 'W_r')}
    del _L2_gnn_all

    def _L3_gnn_setup():
        import jax, jax.numpy as jnp
        import numpy as np
        N_NODES = 10000
        N_EDGES = 5000
        IN_DIM = 512
        OUT_DIM = 512
        LN_EPS = 1e-05
        key = jax.random.key(seed)
        k_x, k_src, k_ws, k_wn = jax.random.split(key, 4)
        x = jax.random.normal(k_x, (N_NODES, IN_DIM), dtype=jnp.float32)
        edge_src = jax.random.randint(k_src, (N_EDGES,), 0, N_NODES, dtype=jnp.int32)
        edge_dst = jnp.repeat(jnp.arange(N_NODES, dtype=jnp.int32), N_EDGES // N_NODES)
        deg = jnp.full((N_NODES,), float(N_EDGES // N_NODES), dtype=jnp.float32)
        scale = 1.0 / np.sqrt(IN_DIM)
        W_self = jax.random.normal(k_ws, (OUT_DIM, IN_DIM), dtype=jnp.float32) * scale
        W_neigh = jax.random.normal(k_wn, (OUT_DIM, IN_DIM), dtype=jnp.float32) * scale
        bias = jnp.zeros((OUT_DIM,), dtype=jnp.float32)
        gamma = jnp.ones((OUT_DIM,), dtype=jnp.float32)
        beta = jnp.zeros((OUT_DIM,), dtype=jnp.float32)
        return {'x': x, 'edge_src': edge_src, 'edge_dst': edge_dst, 'deg': deg, 'W_self': W_self, 'W_neigh': W_neigh, 'bias': bias, 'gamma': gamma, 'beta': beta}
    _L3_gnn_all = _L3_gnn_setup()
    _L3_gnn_in = {k: v for k, v in _L3_gnn_all.items() if k in ('W_self', 'W_neigh', 'bias', 'gamma', 'beta')}
    del _L3_gnn_all
    return {'x': x, 'src': src, 'dst': dst, 'edge_attr_512': edge_attr_512, 'L0_gnn_W': _L0_gnn_in['W'], 'L0_gnn_b': _L0_gnn_in['b'], 'L1_gnn_Wm': _L1_gnn_in['Wm'], 'L1_gnn_bm': _L1_gnn_in['bm'], 'L1_gnn_Wu': _L1_gnn_in['Wu'], 'L1_gnn_bu': _L1_gnn_in['bu'], 'L1_gnn_gamma': _L1_gnn_in['gamma'], 'L1_gnn_beta': _L1_gnn_in['beta'], 'L2_gnn_W_l': _L2_gnn_in['W_l'], 'L2_gnn_b_l': _L2_gnn_in['b_l'], 'L2_gnn_W_r': _L2_gnn_in['W_r'], 'L3_gnn_W_self': _L3_gnn_in['W_self'], 'L3_gnn_W_neigh': _L3_gnn_in['W_neigh'], 'L3_gnn_bias': _L3_gnn_in['bias'], 'L3_gnn_gamma': _L3_gnn_in['gamma'], 'L3_gnn_beta': _L3_gnn_in['beta']}

def reference(x, src, dst, edge_attr_512, L0_gnn_W, L0_gnn_b, L1_gnn_Wm, L1_gnn_bm, L1_gnn_Wu, L1_gnn_bu, L1_gnn_gamma, L1_gnn_beta, L2_gnn_W_l, L2_gnn_b_l, L2_gnn_W_r, L3_gnn_W_self, L3_gnn_W_neigh, L3_gnn_bias, L3_gnn_gamma, L3_gnn_beta):
    import jax
    import jax.numpy as jnp

    def _L0_gnn_ref(x, edge_index, W, b):
        import jax, jax.numpy as jnp
        import numpy as np
        N_NODES = 50000
        N_EDGES = 12500
        IN_DIM = 512
        OUT_DIM = 512
        n = x.shape[0]
        loops = jnp.arange(n, dtype=edge_index.dtype)
        row = jnp.concatenate([edge_index[0], loops])
        col = jnp.concatenate([edge_index[1], loops])
        deg = jax.ops.segment_sum(jnp.ones(row.shape[0], dtype=x.dtype), row, num_segments=n)
        dis = jax.lax.rsqrt(deg)
        norm = dis[row] * dis[col]
        h = x @ W.T + b
        out = jax.ops.segment_sum(norm[:, None] * h[row], col, num_segments=n)
        return jax.nn.relu(out)

    def _L1_gnn_ref(node_tokens, relation_tokens, edge_index, num_nodes, Wm, bm, Wu, bu, gamma, beta):
        import jax, jax.numpy as jnp
        import numpy as np
        N = 10000
        E = 5000
        D = 512
        head = edge_index[0]
        tail = edge_index[1]
        msg = node_tokens[head] + relation_tokens
        msg = msg @ Wm.T + bm
        agg = jax.ops.segment_sum(msg, tail, num_segments=num_nodes)
        deg = jax.ops.segment_sum(jnp.ones((msg.shape[0],), dtype=msg.dtype), tail, num_segments=num_nodes)
        agg = agg / jnp.maximum(deg, 1.0)[:, None]
        update_in = jnp.concatenate((node_tokens, agg), axis=-1)
        update = update_in @ Wu.T + bu
        out = node_tokens + jax.nn.gelu(update, approximate=False)
        mean = jnp.mean(out, axis=-1, keepdims=True)
        var = jnp.var(out, axis=-1, keepdims=True)
        return (out - mean) / jnp.sqrt(var + 1e-05) * gamma + beta

    def _L2_gnn_ref(x, edge_index, W_l, b_l, W_r):
        import jax, jax.numpy as jnp
        import numpy as np
        N_NODES = 10000
        src, dst = (edge_index[0], edge_index[1])
        n = x.shape[0]
        summed = jax.ops.segment_sum(x[src], dst, num_segments=n)
        deg = jax.ops.segment_sum(jnp.ones_like(src, dtype=x.dtype), dst, num_segments=n)
        agg = summed / jnp.maximum(deg, 1.0)[:, None]
        out = agg @ W_l.T + b_l + x @ W_r.T
        out = jax.nn.relu(out)
        return out

    def _L3_gnn_ref(x, edge_src, edge_dst, deg, W_self, W_neigh, bias, gamma, beta):
        import jax, jax.numpy as jnp
        import numpy as np
        N_NODES = 10000
        N_EDGES = 5000
        IN_DIM = 512
        OUT_DIM = 512
        LN_EPS = 1e-05
        n = x.shape[0]
        h_self = jnp.einsum('nd,od->no', x, W_self)
        neigh_sum = jax.ops.segment_sum(x[edge_src], edge_dst, num_segments=n)
        neigh_mean = neigh_sum / jnp.maximum(deg, 1.0)[:, None]
        h_neigh = jnp.einsum('nd,od->no', neigh_mean, W_neigh)
        h = h_self + h_neigh + bias
        mu = jnp.mean(h, axis=-1, keepdims=True)
        var = jnp.mean(jnp.square(h - mu), axis=-1, keepdims=True)
        h = (h - mu) * jax.lax.rsqrt(var + LN_EPS)
        return h * gamma + beta
    edge_index = jnp.stack([src, dst])
    deg = jnp.maximum(jax.ops.segment_sum(jnp.ones(dst.shape, jnp.float32), dst, num_segments=10000), 1.0)
    h = jnp.maximum(_layernorm(x, axis=-1), 0.0)
    x = x + _L0_gnn_ref(h, edge_index, L0_gnn_W, L0_gnn_b)
    h = jnp.maximum(_layernorm(x, axis=-1), 0.0)
    x = x + _L1_gnn_ref(h, edge_attr_512, edge_index, 10000, L1_gnn_Wm, L1_gnn_bm, L1_gnn_Wu, L1_gnn_bu, L1_gnn_gamma, L1_gnn_beta)
    h = jnp.maximum(_layernorm(x, axis=-1), 0.0)
    x = x + _L2_gnn_ref(h, edge_index, L2_gnn_W_l, L2_gnn_b_l, L2_gnn_W_r)
    h = jnp.maximum(_layernorm(x, axis=-1), 0.0)
    x = x + _L3_gnn_ref(h, src, dst, deg, L3_gnn_W_self, L3_gnn_W_neigh, L3_gnn_bias, L3_gnn_gamma, L3_gnn_beta)
    return x

_drawn_inputs = setup_inputs


def setup_inputs(seed=0):
    import zlib

    import numpy as np

    out = dict(_drawn_inputs(seed))
    spreads = {'L1_gnn_bm': (0.0, 0.343),
     'L1_gnn_bu': (0.0, 0.1),
     'L1_gnn_gamma': (1.0, 0.2),
     'L1_gnn_beta': (0.0, 0.1),
     'L3_gnn_bias': (0.0, 0.1),
     'L3_gnn_gamma': (1.0, 0.2),
     'L3_gnn_beta': (0.0, 0.1)}
    factors = {'L0_gnn_b': 7.324, 'L2_gnn_b_l': 4.69}
    for name, (base, spread) in spreads.items():
        noise = np.random.default_rng([zlib.crc32(name.encode()), seed]).standard_normal(out[name].shape)
        drawn = base * np.exp(spread * noise) if base else spread * noise
        out[name] = jnp.asarray(drawn.astype(out[name].dtype))
    for name, factor in factors.items():
        out[name] = (out[name] * factor).astype(out[name].dtype)
    return out
```

```python
import concourse.bass as bass
from concourse import mybir
from concourse.alu_op_type import AluOpType as ALU
from contextlib import ExitStack
import numpy as np

FP32 = mybir.dt.float32
FP16 = mybir.dt.float16
BF16 = mybir.dt.bfloat16
INT32 = mybir.dt.int32
ACT = mybir.ActivationFunctionType
AX_X = mybir.AxisListType.X

P = 128
N = 10000
E = 10000
D = 512
KD = D // P
NT = -(-N // P)
LAST = N - (NT - 1) * P
NPAD = NT * P
PAIRS = NT // 2
NJ = NT + 1
EP, ET = 125, 80
RING = 4
NC = -(-(NT + E // P) // RING) * RING
LAG = 2
NOWHERE = 1 << 20
TW0 = 2 * D + 16
EPS = 1e-5
ASCALE = 1024.0


def gnn_kernel(nc, x, src, dst, edge_attr, W0, b0, Wm, bm, Wu, bu, g1, be1, Wl, bl, Wr, Wself, Wneigh,
               bias3, g3, be3, out):
    dram = nc.dram_tensor
    tables = [dram("table0", [NPAD, TW0], FP16).ap()] + [
        dram(f"table{n}", [NPAD, 2 * D], FP16).ap() for n in (1, 2, 3)]
    xs = [x] + [dram(f"x{n}", [NPAD, D], FP32).ap() for n in (1, 2, 3)]
    records = dram("records", [P * NC, 4], INT32).ap()
    widths = [TW0, 2 * D, 2 * D, 2 * D]

    ctx = ExitStack()
    with ctx:
        def sb(name, shape, dt):
            return ctx.enter_context(nc.sbuf_tensor(name, shape, dt))

        def sem(name):
            return ctx.enter_context(nc.semaphore(name))

        NAMES = ["W0", "Wu1", "Wr", "Wl", "Wself", "Wneigh"]
        whi = {n: sb(f"{n}_hi", [P, KD, D], FP16) for n in NAMES}
        wlo = {n: sb(f"{n}_lo", [P, KD, D], FP16) for n in NAMES}
        wc = sb("wc", [P, KD, D], FP32)
        unscale = sb("unscale", [P, len(NAMES)], FP32)
        wscale = sb("wscale", [P, len(NAMES)], FP32)
        wmax = sb("wmax", [P, len(NAMES)], FP32)
        wmaxall = sb("wmaxall", [P, len(NAMES)], FP32)
        wexp = sb("wexp", [P, 4], INT32)
        UN = {n: unscale[:, i:i + 1] for i, n in enumerate(NAMES)}
        rows = {n: sb(f"row_{n}", [P, D], FP32) for n in
                ["b0", "bu", "g1", "be1", "bl", "bias3", "g3", "be3", "vb"]}
        bmcol = sb("bmcol", [P, KD], FP32)
        bmwide = sb("bmwide", [P, KD, P], FP32)

        select = sb("select", [P, NC * P], FP16)
        JB, PB = NJ * ET, ET * P
        tile_hot = select[:, 0:JB]
        row_hot = select[:, JB:JB + PB]
        room = sb("room", [P, 9600], FP32)
        before = room[:, 0:JB // 2].bitcast(BF16)
        summed = room[:, JB // 2:JB // 2 + JB]
        notfirst = room[:, JB // 2:JB].bitcast(BF16)
        o = RING * TW0 // 2
        ring = room[:, 0:o].bitcast(FP16)
        o += 0
        pieces = room[:, o:o + RING * 3 * D // 2].bitcast(BF16)
        o += RING * 3 * D // 2
        eraw = [room[:, o + D * s:o + D * (s + 1)] for s in range(2)]
        o += 2 * D
        escaled = room[:, o:o + D]
        eres = room[:, o + D:o + 2 * D]
        o += 2 * D
        RINGS = o
        gbuf, habuf, xn0, xn1 = [room[:, o + D * n:o + D * (n + 1)] for n in range(4)]
        xnew = [xn0, xn1]
        assert o + 4 * D <= 9600 and JB // 2 + JB <= 9600

        ends = sb("ends", [P, 2, ET], INT32)
        tmpi = sb("tmpi", [P, ET], INT32)
        tilef = sb("tilef", [P, ET], FP32)
        rowf = sb("rowf", [P, ET], FP32)
        rowtot = sb("rowtot", [P, NJ], BF16)
        slotf = sb("slotf", [P, ET], FP32)
        sloti = sb("sloti", [P, ET], INT32)
        slotp = sb("slotp", [P, ET], INT32)
        slotc = sb("slotc", [P, ET], INT32)
        slotrow = sb("slotrow", [P, ET], INT32)
        rec = sb("rec", [P, ET, 4], INT32)
        nowhere = sb("nowhere", [P, NC * 4], INT32)
        recback = sb("recback", [P, NC + 1, 4], INT32)
        relf = sb("relf", [P, NC], FP32)
        idx = sb("idx", [P, RING], INT32)
        idxe = sb("idxe", [P, RING], INT32)
        kf = sb("kf", [P, NJ], FP32)
        ki = sb("ki", [P, NJ], INT32)
        cincl = sb("cincl", [P, NJ], FP32)
        cexcl = sb("cexcl", [P, NJ], FP32)
        cbase = sb("cbase", [P, NJ], FP32)
        cfirst = sb("cfirst", [1, NJ], INT32)
        deg = sb("deg", [P, NJ], FP32)
        degmax = sb("degmax", [P, NJ], FP32)
        dexp = sb("dexp", [P, NJ], INT32)
        down = sb("down", [P, NJ], FP32)
        up = sb("up", [P, NJ], FP32)
        indeg1 = sb("indeg1", [P, NJ], FP32)
        has = sb("has", [P, NJ], FP32)
        rdeg = sb("rdeg", [P, NJ], FP32)
        rt = [sb(f"rt{n}", [P, NJ], FP32) for n in range(4)]
        dis = sb("dis", [P, NJ], FP32)
        sqd = sb("sqd", [P, NJ], FP32)
        dis1k = sb("dis1k", [P, NJ], FP32)
        dishl = sb("dishl", [P, NJ, 2], FP16)

        iota_j = sb("iota_j", [P, NJ], FP32)
        iota_p = sb("iota_p", [P, P], FP32)
        ident = sb("ident", [P, P], FP32)
        identh = sb("identh", [P, P], FP16)
        earlier = sb("earlier", [P, P], BF16)
        onesb = sb("onesb", [P, P], BF16)
        zeros = sb("zeros", [P, P], FP16)
        ones_j = sb("ones_j", [P, NJ], FP32)
        eps1 = sb("eps1", [P, 1], FP32)
        eps1k = sb("eps1k", [P, 1], FP32)

        stage = sb("stage", [P, 10 * D], FP32)
        wst = [stage[:, 2048 * s:2048 * (s + 1)] for s in range(2)]
        hrow = [stage[:, D * s:D * (s + 1)].bitcast(FP16) for s in range(2)]
        hT = [stage[:, D * (2 + s):D * (3 + s)].bitcast(FP16) for s in range(2)]
        aggT = [stage[:, D * (4 + s):D * (5 + s)] for s in range(2)]
        aggh = [a.bitcast(FP16) for a in aggT]
        tbuf = stage[:, D * 6:D * 7]
        t2buf = stage[:, D * 7:D * 8]
        ubuf = [stage[:, D * (8 + s):D * (9 + s)] for s in range(2)]
        xbuf = [sb(f"xbuf{s}", [P, D], FP32) for s in range(2)]
        h32 = [sb(f"h32{s}", [P, D], FP32) for s in range(2)]
        hout = [sb(f"hout{s}", [P, TW0], FP16) for s in range(2)]
        stats = sb("stats", [P, 6], FP32)
        mv = [sb(f"mv{s}", [P, 2], FP32) for s in range(2)]
        mv2 = sb("mv2", [P, 2], FP32)
        std = [sb(f"std{s}", [P, 1], FP32) for s in range(2)]
        std2 = sb("std2", [P, 1], FP32)
        rstd2 = sb("rstd2", [P, 1], FP32)
        rstd = sb("rstd", [P, NJ], FP32)
        nbias = sb("nbias", [P, NJ], FP32)
        s1 = sb("s1", [P, 1], FP32)
        s2 = [sb(f"s2{s}", [P, 1], FP32) for s in range(2)]
        rtmp = sb("rtmp", [P, 1], FP32)

        bank = [ctx.enter_context(nc.psum_tensor(f"bank{i}", [P, D], FP32)) for i in range(8)]
        p_T = bank[0][:, :].bitcast(FP16)
        p_norm = bank[1]
        p_agg = [bank[2], bank[3]]
        p_self = [bank[4], bank[5]]
        p_out = [bank[6], bank[7]]

        q_const = sem("q_const")
        q_ends = sem("q_ends")
        q_w = [sem(f"q_w{s}") for s in range(2)]
        q_rows = sem("q_rows")
        q_order = sem("q_order")
        q_hot = sem("q_hot")
        q_deg = sem("q_deg")
        q_rowtot = sem("q_rowtot")
        q_base = sem("q_base")
        q_sq = sem("q_sq")
        q_sqin = sem("q_sqin")
        q_degsb = sem("q_degsb")
        q_degmax = sem("q_degmax")
        q_slot = sem("q_slot")
        q_fill = sem("q_fill")
        q_scat = sem("q_scat")
        q_rec = sem("q_rec")
        q_sel = sem("q_sel")
        q_cf = sem("q_cf")
        q_wmax = sem("q_wmax")
        q_wmaxall = sem("q_wmaxall")
        q_wsc = sem("q_wsc")
        q_wT = sem("q_wT")
        q_whi = sem("q_whi")
        q_wlo = sem("q_wlo")
        q_bmw = sem("q_bmw")
        q_wu2 = sem("q_wu2")
        q_wc = sem("q_wc")
        q_wcs = sem("q_wcs")
        q_clean = sem("q_clean")
        q_ready = sem("q_ready")

        x_loaded = [sem(f"x_loaded{s}") for s in range(2)]
        x_used = sem("x_used")
        h_loaded = [sem(f"h_loaded{s}") for s in range(2)]
        h_used = sem("h_used")
        gathered = [sem(f"gathered{r}") for r in range(RING)]
        egathered = [sem(f"egathered{r}") for r in range(2)]
        idx_set = sem("idx_set")
        eidx_set = sem("eidx_set")
        e_step = sem("e_step")
        landed = sem("landed")
        chunk_used = sem("chunk_used")
        hT_ps = sem("hT_ps")
        hT_sb = sem("hT_sb")
        agg_ps = sem("agg_ps")
        agg_hi = sem("agg_hi")
        agg_lo = sem("agg_lo")
        out_ps = sem("out_ps")
        mixed = sem("mixed")
        norm_in = sem("norm_in")
        brow = sem("brow")
        u_ready = sem("u_ready")
        g_ready = sem("g_ready")
        g_used = sem("g_used")
        var2 = sem("var2")
        std2_ready = sem("std2_ready")
        var1 = sem("var1")
        std1 = sem("std1")
        scale1 = sem("scale1")
        hi_ready = sem("hi_ready")
        lo_ready = sem("lo_ready")
        stored = [sem(f"stored{s}") for s in range(2)]
        passed = sem("passed")
        step = sem("step")

        block = ctx.enter_context(nc.Block())

        def apart(eng):
            eng.sem_inc(passed, 1)

        def tiles(eng, body):
            with eng.Fori(0, PAIRS) as i:
                body(2 * i, 0, False)
                body(2 * i + 1, 1, False)
            body(NT - 1, 0, True)

        def in_slot(ph, t, s):
            per = (NT + 1) // 2 if s == 0 else NT // 2
            if isinstance(t, int):
                return ph * per + t // 2
            return ph * per + (t - s) // 2

        def half(t, s):
            return (t - s) // 2

        def nrows(last, rows_ap, t):
            return rows_ap[(NT - 1) * P:N, :] if last else rows_ap[bass.ds(t * P, P), :]

        @block.sync
        def _(sp):
            sp.dma_start(ends[0:EP, 0, :], src.rearrange("(p t) -> p t", t=ET)).then_inc(q_ends, 16)
            sp.dma_start(ends[0:EP, 1, :], dst.rearrange("(p t) -> p t", t=ET)).then_inc(q_ends, 16)
            for n, v in (("b0", b0), ("bu", bu), ("g1", g1), ("be1", be1), ("bl", bl), ("bias3", bias3),
                         ("g3", g3), ("be3", be3)):
                sp.dma_start(rows[n][:, :], v[None, :].broadcast_to([P, D])).then_inc(q_rows, 16)
            sp.dma_start(bmcol[:, :], bm.rearrange("(k p) -> p k", p=P),
                         allow_slow_non_contiguous=True).then_inc(q_rows, 16)
            mats = [W0, Wu[:, 0:D], Wr, Wl, Wself, Wneigh, Wu[:, D:2 * D], Wm]
            for n, w in enumerate(mats):
                if n >= 2 and n < 7:
                    sp.wait_ge(q_wlo, KD * (n - 1))
                if n == 7:
                    sp.wait_ge(q_wlo, KD * 6)
                sp.dma_start(wst[n % 2].rearrange("p (b d) -> p b d", b=KD),
                             w.rearrange("(b p) d -> p b d", p=P)).then_inc(q_w[n % 2], 16)

            def first_x(t, s, last):
                sp.wait_ge(x_used, t + 1)
                if last:
                    sp.dma_start(xbuf[s][0:LAST, :], nrows(True, x, t)).then_inc(x_loaded[s], 16)
                else:
                    sp.dma_start(xbuf[s][:, :], nrows(False, x, t)).then_inc(x_loaded[s], 16)
            tiles(sp, first_x)

            sp.wait_ge(q_scat, 16 * ET)
            sp.dma_start(recback[:, 0:NC, :].rearrange("p c w -> p (c w)"),
                         records.rearrange("(p c) w -> p (c w)", p=P)).then_inc(q_rec, 16)
            sp.wait_ge(q_ready, 2)
            for L in range(4):
                for s in range(2):
                    sp.wait_ge(stored[s], 16 * (in_slot(1, 0, s) + L * 2 * in_slot(1, 0, s)))

                def load(t, s, last):
                    sp.wait_ge(h_used, NT * L + t + 1)
                    sp.dma_start(hrow[s][:, :], tables[L][bass.ds(t * P, P), 0:2 * D]
                                 ).then_inc(h_loaded[s], 16)
                    sp.wait_ge(x_used, NT * (L + 1) + t + 1)
                    if last and L == 0:
                        sp.dma_start(xbuf[s][0:LAST, :], nrows(True, x, t)).then_inc(x_loaded[s], 16)
                    else:
                        sp.dma_start(xbuf[s][:, :], xs[L][bass.ds(t * P, P), :]).then_inc(x_loaded[s], 16)
                tiles(sp, load)

        @block.gpsimd
        def _(pool):
            g = nc.gpsimd
            g.iota(iota_j[:, :], [[1, NJ]], base=0, channel_multiplier=0, allow_small_or_imprecise_dtypes=True)
            g.iota(iota_p[:, :], [[1, P]], base=0, channel_multiplier=0, allow_small_or_imprecise_dtypes=True)
            g.memset(nowhere[:, :], NOWHERE)
            g.memset(recback[:, NC, :], NOWHERE)
            g.memset(ident[:, :], 0.0)
            g.memset(identh[:, :], 0.0)
            g.memset(onesb[:, :], 1.0)
            g.memset(ones_j[:, :], 1.0)
            g.memset(zeros[:, :], 0.0)
            g.memset(eps1[:, :], EPS)
            g.memset(eps1k[:, :], EPS / ASCALE ** 2)
            g.memset(hout[0][:, :], 0.0)
            g.memset(hout[1][:, :], 0.0)
            nf = notfirst.rearrange("p (j t) -> p j t", t=ET)
            g.memset(notfirst, 1.0)
            g.memset(earlier[:, :], 1.0).then_inc(q_const, 1)
            pool.wait_ge(q_const, 1)
            g.memset(nf[:, :, 0:1], 0.0)
            g.iota(rec[0:EP, :, 1], [[1, ET]], base=0, channel_multiplier=ET)
            g.affine_select(out=earlier[:, :], in_=earlier[:, :], compare_op=ALU.is_gt, fill=0.0, base=0,
                            pattern=[[1, P]], channel_multiplier=-1)
            g.affine_select(out=ident[:, :], in_=ident[:, :], compare_op=ALU.not_equal, fill=1.0, base=0,
                            pattern=[[-1, P]], channel_multiplier=1)
            g.affine_select(out=identh[:, :], in_=identh[:, :], compare_op=ALU.not_equal, fill=1.0, base=0,
                            pattern=[[-1, P]], channel_multiplier=1).then_inc(q_const, 1)
            pool.wait_ge(q_degsb, 1)
            g.partition_all_reduce(degmax[:, :], indeg1[:, :], P, bass.bass_isa.ReduceOp.max
                                   ).then_inc(q_degmax, 1)
            for n in range(len(NAMES)):
                pool.wait_ge(q_wmax, n + 1)
                g.partition_all_reduce(wmaxall[:, n:n + 1], wmax[:, n:n + 1], P,
                                       bass.bass_isa.ReduceOp.max).then_inc(q_wmaxall, 1)
            pool.wait_ge(q_fill, 16)
            pool.wait_ge(q_slot, 1)
            for t in range(ET):
                g.indirect_dma_start(out=records, out_offset=bass.IndirectOffsetOnAxis(ap=slotrow[0:EP, t:t + 1], axis=0),
                                     in_=rec[0:EP, t, :], in_offset=None).then_inc(q_scat, 16)
            g.memset(room[:, 0:RINGS], 0.0).then_inc(q_clean, 1)
            pool.wait_ge(q_clean, 1)
            pool.wait_ge(q_sel, 1)

            for L in range(4):
                for s in range(2):
                    pool.wait_ge(stored[s], 16 * (in_slot(1, 0, s) + L * 2 * in_slot(1, 0, s)))
                per = NC // RING
                W = widths[L]

                def edges(c, r):
                    g.tensor_copy(idxe[:, r:r + 1], recback[:, bass.ds(c, 1), 1]).then_inc(eidx_set, 1)
                    pool.wait_ge(eidx_set, c + 1)
                    apart(pool)
                    g.indirect_dma_start(
                        out=eraw[r % 2], out_offset=None, in_=edge_attr,
                        in_offset=bass.IndirectOffsetOnAxis(ap=idxe[:, r:r + 1], axis=0),
                        bounds_check=E - 1, oob_is_err=False).then_inc(egathered[r % 2], 16)

                if L == 1:
                    edges(0, 0)
                with pool.Fori(0, per) as i:
                    for r in range(RING):
                        c = RING * i + r
                        pool.wait_ge(chunk_used, NC * L + c + 1)
                        apart(pool)
                        g.tensor_copy(idx[:, r:r + 1], recback[:, bass.ds(c, 1), 0]).then_inc(idx_set, 1)
                        pool.wait_ge(idx_set, NC * L + c + 1)
                        apart(pool)
                        g.indirect_dma_start(
                            out=ring[:, r * TW0:r * TW0 + W], out_offset=None, in_=tables[L],
                            in_offset=bass.IndirectOffsetOnAxis(ap=idx[:, r:r + 1], axis=0),
                            bounds_check=NPAD - 1, oob_is_err=False).then_inc(gathered[r], 16)
                        if L == 1:
                            edges(c + 1, (r + 1) % RING)
                            pool.wait_ge(egathered[r % 2], 16 * (2 * i + r // 2 + 1))
                            apart(pool)
                            part = [pieces[:, (3 * r + k) * D:(3 * r + k + 1) * D] for k in range(3)]
                            n0 = 5 * c
                            g.tensor_scalar(escaled, eraw[r % 2], ASCALE, None, ALU.mult).then_inc(e_step, 1)
                            pool.wait_ge(e_step, n0 + 1)
                            apart(pool)
                            g.tensor_copy(part[0], escaled).then_inc(e_step, 1)
                            pool.wait_ge(e_step, n0 + 2)
                            g.tensor_tensor(eres, escaled, part[0], ALU.subtract).then_inc(e_step, 1)
                            pool.wait_ge(e_step, n0 + 3)
                            apart(pool)
                            g.tensor_copy(part[1], eres).then_inc(e_step, 1)
                            pool.wait_ge(e_step, n0 + 4)
                            g.tensor_tensor(part[2], eres, part[1], ALU.subtract).then_inc(e_step, 1)
                            pool.wait_ge(e_step, n0 + 5)
                            pool.wait_ge(gathered[r], 16 * (per * L + i + 1))
                            apart(pool)
                            pool.sem_inc(landed, 1)
                        else:
                            b = (r - LAG) % RING
                            n = per * L + i + (1 if r >= LAG else 0)
                            pool.wait_ge(gathered[b], 16 * n)
                            apart(pool)
                            pool.sem_inc(landed, 1)
                if L == 1:
                    pool.wait_ge(egathered[0], 16 * (2 * per + 1))
                else:
                    for r in range(RING - LAG, RING):
                        pool.wait_ge(gathered[r], 16 * per * (L + 1))
                        pool.sem_inc(landed, 1)

        def landed_for(L, c):
            base = NC * L + LAG * (L - (1 if L > 1 else 0))
            return base + c + 1 + (0 if L == 1 else LAG)

        @block.tensor
        def _(pe):
            mm = nc.tensor.matmul
            pe.sem_inc(chunk_used, RING)
            pe.sem_inc(h_used, 2)
            pe.wait_ge(q_const, 2)
            th = tile_hot[0:EP, :].rearrange("p (j t) -> p j t", t=ET)
            rh = row_hot[0:EP, :].rearrange("p (t r) -> p t r", r=P)
            for n in range(2):
                pe.wait_ge(q_hot, n + 1)
                for t in range(ET):
                    last = mm(p_self[n][:, 0:NJ], rh[:, t, :], th[:, :, t], start=(t == 0), stop=(t == ET - 1))
                last.then_inc(q_deg, 1)
            pe.wait_ge(q_rowtot, 1)
            mm(p_out[0][0:EP, 0:NJ], earlier[0:EP, 0:EP], rowtot[0:EP, :], start=True, stop=True)
            mm(p_out[1][:, 0:NJ], onesb[0:EP, :], rowtot[0:EP, :], start=True, stop=True).then_inc(q_base, 1)
            for n in range(7):
                w = wst[n % 2].rearrange("p (b d) -> p b d", b=KD)
                pe.wait_ge(q_w[n % 2], 16 * (n // 2 + 1))
                for k in range(KD):
                    m = KD * n + k
                    if m >= 2:
                        pe.wait_ge(q_whi, m - 1)
                        if m - 2 < KD * 6:
                            pe.wait_ge(q_wlo, m - 1)
                        else:
                            pe.wait_ge(q_wlo, KD * 6)
                    for b in range(KD):
                        last = nc.tensor.transpose(p_agg[m % 2][:, b * P:(b + 1) * P], w[:, b, k * P:(k + 1) * P],
                                                   ident[:, :])
                    last.then_inc(q_wT, 1)
            wu2T = wst[0].rearrange("p (k o) -> p k o", k=KD)
            wmn = wst[1].rearrange("p (b d) -> p b d", b=KD)
            pe.wait_ge(q_w[1], 16 * 4)
            pe.wait_ge(q_wu2, KD)
            pe.wait_ge(q_bmw, 1)
            for k in range(KD):
                if k >= 2:
                    pe.wait_ge(q_wcs, k - 1)
                for b in range(KD):
                    last = mm(p_agg[k % 2][:, :], wmn[:, b, k * P:(k + 1) * P], wu2T[:, b, :],
                              start=(b == 0), stop=(b == KD - 1))
                last.then_inc(q_wc, 1)
            pe.wait_ge(q_wcs, 3)
            for b in range(KD):
                last = mm(p_agg[0][:, :], bmwide[:, b, :], wu2T[:, b, :], start=(b == 0), stop=(b == KD - 1))
            last.then_inc(q_wc, 1)
            pe.wait_ge(q_cf, 1)
            pe.wait_ge(q_sel, 1)
            pe.wait_ge(q_wcs, 5)

            selfW = [None, "Wu1", "Wr", "Wself"]
            aggW = ["W0", None, "Wl", "Wneigh"]

            for L in range(4):
                def gather_sum(t, s):
                    pe.wait_ge(h_loaded[s], 16 * (in_slot(L, t, s) + 1))
                    if L > 0:
                        if isinstance(t, int) and t == 0:
                            pe.wait_ge(hT_sb, NT * (L - 1))
                        else:
                            pe.wait_ge(hT_sb, NT * (L - 1) + t)
                        for k in range(2 * KD):
                            last = nc.tensor.transpose(p_T[:, k * P:(k + 1) * P], hrow[s][:, k * P:(k + 1) * P],
                                                       identh[:, :])
                        last.then_inc(hT_ps, 1)
                    pa = p_agg[s]
                    n_lo = L - (1 if L > 1 else 0)
                    if L == 1:
                        pe.wait_ge(agg_hi, NT * L + t + 1)
                    else:
                        pe.wait_ge(agg_lo, NT * n_lo + t + 1)
                        pe.wait_ge(agg_hi, NT * L + t + 1)
                    if L == 0:
                        pe.wait_ge(norm_in, t + 1)
                        mm(p_norm[:, 8 * s:8 * s + 1], zeros[:, :], zeros[:, 0:1], start=True, stop=False,
                           skip_group_check=True)
                    opened = mm(pa[:, 0:1], zeros[:, :], zeros[:, 0:1], start=True, stop=False,
                                skip_group_check=True)
                    if L > 0:
                        opened.then_inc(h_used, 1)
                    if L == 0:
                        for half_ in range(2):
                            for k in range(KD):
                                last = mm(pa[:, k * P:(k + 1) * P], hrow[s][:, half_ * D + k * P:half_ * D + (k + 1) * P],
                                          identh[:, :], start=False, stop=False, skip_group_check=True)
                        last.then_inc(h_used, 1)
                    first = pe.value_load(cfirst[0:1, bass.ds(t, 1)], min_val=0, max_val=NC - 1)
                    after = pe.value_load(cfirst[0:1, bass.ds(t + 1, 1)], min_val=1, max_val=NC)
                    with pe.Fori(first, after) as c:
                        pe.wait_ge(landed, landed_for(L, c))
                        r = c % RING
                        sel = select[:, bass.ds(c * P, P)]
                        base = r * TW0
                        for half_ in range(2):
                            for k in range(KD):
                                last = mm(pa[:, k * P:(k + 1) * P],
                                          ring[:, bass.ds(base + (half_ * D + k * P), P)], sel,
                                          start=False, stop=False, skip_group_check=True)
                        if L == 0:
                            for q in range(2):
                                last = mm(p_norm[:, 8 * s:8 * s + 1], sel, ring[:, bass.ds(base + (2 * D + q), 1)],
                                          start=False, stop=False, skip_group_check=True)
                        if L == 1:
                            for q in range(3):
                                for k in range(KD):
                                    last = mm(pa[:, k * P:(k + 1) * P],
                                              pieces[:, bass.ds(r * (3 * D) + (q * D + k * P), P)], sel,
                                              start=False, stop=False, skip_group_check=True)
                        last.then_inc(chunk_used, 1)
                    if L == 0:
                        mm(p_norm[:, 8 * s:8 * s + 1], zeros[:, :], zeros[:, 0:1], start=False, stop=True,
                           skip_group_check=True)
                    mm(pa[:, 0:1], zeros[:, :], zeros[:, 0:1], start=False, stop=True,
                       skip_group_check=True).then_inc(agg_ps, 1)

                def products(t, s):
                    pe.wait_ge(mixed, NT * L + t + 1)
                    if L > 0:
                        pe.wait_ge(hT_sb, NT * (L - 1) + t + 1)
                        hi, lo = whi[selfW[L]], wlo[selfW[L]]
                        for k in range(KD):
                            a, b = hT[s][:, k * P:(k + 1) * P], hT[s][:, D + k * P:D + (k + 1) * P]
                            mm(p_self[s][:, :], a, hi[:, k, :], start=(k == 0), stop=False)
                            mm(p_self[s][:, :], a, lo[:, k, :], start=False, stop=False)
                            mm(p_self[s][:, :], b, hi[:, k, :], start=False, stop=(k == KD - 1))
                    pe.wait_ge(agg_hi, NT * L + t + 3)
                    if L == 1:
                        for k in range(KD):
                            last = mm(p_out[s][:, :], aggT[s][:, k * P:(k + 1) * P], wc[:, k, :],
                                      start=(k == 0), stop=(k == KD - 1))
                    else:
                        pe.wait_ge(agg_lo, NT * (L - (1 if L > 1 else 0)) + t + 3)
                        hi, lo = whi[aggW[L]], wlo[aggW[L]]
                        for k in range(KD):
                            a, b = aggh[s][:, k * P:(k + 1) * P], aggh[s][:, D + k * P:D + (k + 1) * P]
                            mm(p_out[s][:, :], a, hi[:, k, :], start=(k == 0), stop=False)
                            mm(p_out[s][:, :], a, lo[:, k, :], start=False, stop=False)
                            last = mm(p_out[s][:, :], b, hi[:, k, :], start=False, stop=(k == KD - 1))
                    last.then_inc(out_ps, 1)

                gather_sum(0, 0)
                with pe.Fori(0, PAIRS) as i:
                    gather_sum(2 * i + 1, 1)
                    products(2 * i, 0)
                    gather_sum(2 * i + 2, 0)
                    products(2 * i + 1, 1)
                products(NT - 1, 0)

        @block.scalar
        def _(act):
            f = nc.scalar.activation
            act.wait_ge(q_const, 1)
            act.dma_start(records.rearrange("(p c) w -> p (c w)", p=P), nowhere[:, :]).then_inc(q_fill, 16)
            act.wait_ge(q_sqin, 1)
            f(sqd[:, :], dis[:, :], ACT.Sqrt).then_inc(q_sq, 1)
            act.wait_ge(q_rows, 16 * 9)
            for k in range(KD):
                last = f(bmwide[:, k, :], zeros[:, :], ACT.Identity, bias=bmcol[:, k:k + 1])
            last.then_inc(q_bmw, 1)
            for n in range(7):
                for k in range(KD):
                    m = KD * n + k
                    act.wait_ge(q_wT, m + 1)
                    if n < 6:
                        act.wait_ge(q_wsc, n + 1)
                        f(whi[NAMES[n]][:, k, :], p_agg[m % 2][:, :], ACT.Copy,
                          scale=wscale[:, n:n + 1]).then_inc(q_whi, 1)
                    else:
                        f([ubuf[0], ubuf[1], gbuf[:, :], habuf[:, :]][k], p_agg[m % 2][:, :], ACT.Copy).then_inc(q_whi, 1)
            act.wait_ge(q_whi, KD * 7)
            for k in range(KD):
                f(wst[0][:, k * D:(k + 1) * D], [ubuf[0], ubuf[1], gbuf[:, :], habuf[:, :]][k], ACT.Copy).then_inc(q_wu2, 1)
            for k in range(KD):
                act.wait_ge(q_wc, k + 1)
                f(wc[:, k, :], p_agg[k % 2][:, :], ACT.Copy).then_inc(q_wcs, 1)
            act.wait_ge(q_wc, KD + 1)
            f(rows["vb"][:, :], p_agg[0][:, :], ACT.Copy).then_inc(q_wcs, 1)
            act.wait_ge(q_wcs, 5)
            act.sem_inc(q_ready, 1)
            act.sem_inc(agg_hi, 2)

            def std_of_new(ph, t, s):
                act.wait_ge(var1, NT * ph + t + 1)
                f(std[s][:, :], mv[s][:, 1:2], ACT.Sqrt, scale=1 / ASCALE ** 2, bias=eps1k[:, :]).then_inc(std1, 1)

            def normalise(ph, t, s, xn):
                act.wait_ge(scale1, NT * ph + t + 1)
                act.wait_ge(lo_ready, NT * ph + t + 1)
                act.wait_ge(stored[s], 16 * stores(ph, t, s))
                apart(act)
                sc, bi = rstd[:, bass.ds(t, 1)], nbias[:, bass.ds(t, 1)]
                f(h32[s][:, :], xn[s][:, :], ACT.Relu, scale=sc, bias=bi)
                f(hout[s][:, 0:D], xn[s][:, :], ACT.Relu, scale=sc, bias=bi).then_inc(hi_ready, 1)

            def stores(ph, t, s):
                per = (NT + 1) // 2 if s == 0 else NT // 2
                return 0 if ph == -1 else (half(t, s) if ph == 0 else per + (ph - 1) * 2 * per + 2 * half(t, s))

            def store(ph, t, s):
                act.wait_ge(lo_ready, NT * ph + t + 3)
                w = widths[ph]
                act.dma_start(tables[ph][bass.ds(t * P, P), :], hout[s][:, 0:w]).then_inc(stored[s], 16)
                if ph > 0:
                    act.dma_start(xs[ph][bass.ds(t * P, P), :], xnew[s][:, :]).then_inc(stored[s], 16)

            def phase0(t, s, last):
                std_of_new(0, t, s)
                normalise(0, t, s, xbuf)
                store(0, t, s)
            tiles(act, phase0)

            for L in range(4):
                ph = L + 1

                def evacuate(t, s):
                    if L > 0:
                        act.wait_ge(hT_ps, NT * (L - 1) + t + 1)
                        act.wait_ge(out_ps, NT * L + t - 1 if L > 0 else 0)
                        f(hT[s][:, :], p_T, ACT.Copy).then_inc(hT_sb, 1)
                    act.wait_ge(agg_ps, NT * L + t + 1)
                    if L == 1:
                        f(aggT[s], p_agg[s][:, :], ACT.Copy).then_inc(agg_hi, 1)
                    else:
                        act.wait_ge(mixed, NT * L + t + 1)
                        apart(act)
                        f(aggh[s][:, 0:D], p_agg[s][:, :], ACT.Copy, scale=down[:, bass.ds(t, 1)]).then_inc(agg_hi, 1)

                def epilogue(t, s, last):
                    if L == 0:
                        act.wait_ge(norm_in, t + 3)
                        act.wait_ge(mixed, t + 2)
                        f(tbuf, rows["b0"][:, :], ACT.Copy, scale=s2[s][:, :]).then_inc(brow, 1)
                    if L == 1:
                        act.wait_ge(u_ready, t + 1)
                        act.wait_ge(g_used, t)
                        f(gbuf[:, :], ubuf[s], ACT.Gelu)
                        act.wait_ge(x_loaded[s], 16 * (in_slot(ph, t, s) + 1))
                        f(habuf[:, :], xbuf[s][:, :], ACT.Relu, scale=rstd[:, bass.ds(t, 1)],
                          bias=nbias[:, bass.ds(t, 1)]).then_inc(g_ready, 1)
                    if L in (1, 3):
                        act.wait_ge(var2, NT * (L // 2) + t + 1)
                        f(std2[:, :], mv2[:, 1:2], ACT.Sqrt, bias=eps1[:, :]).then_inc(std2_ready, 1)
                    if L < 3:
                        std_of_new(ph, t, s)
                        normalise(ph, t, s, xnew)
                        store(ph, t, s)
                    else:
                        act.wait_ge(var1, NT * ph + t + 1)
                        if last:
                            act.dma_start(nrows(True, out, t), xnew[s][0:LAST, :]).then_inc(stored[s], 16)
                        else:
                            act.dma_start(nrows(False, out, t), xnew[s][:, :]).then_inc(stored[s], 16)

                evacuate(0, 0)
                with act.Fori(0, PAIRS) as i:
                    evacuate(2 * i + 1, 1)
                    epilogue(2 * i, 0, False)
                    evacuate(2 * i + 2, 0)
                    epilogue(2 * i + 1, 1, False)
                epilogue(NT - 1, 0, True)
            for s in range(2):
                act.wait_ge(stored[s], 16 * (stores(4, s, s) + in_slot(1, 0, s)))

        @block.vector
        def _(dve):
            v = nc.vector
            v.memset(s1[:, :], 0.0)
            dve.sem_inc(x_used, 2)
            dve.sem_inc(mixed, 2)
            dve.sem_inc(agg_lo, 2)
            dve.sem_inc(norm_in, 2)
            dve.sem_inc(lo_ready, 2)
            made = [0]

            def link(ins):
                made[0] += 1
                ins.then_inc(q_order, 1)
                dve.wait_ge(q_order, made[0])

            dve.wait_ge(q_const, 2)
            dve.wait_ge(q_ends, 32)
            th = tile_hot[0:EP, :].rearrange("p (j t) -> p j t", t=ET)
            rh = row_hot[0:EP, :].rearrange("p (t r) -> p t r", r=P)

            def one_hots(n):
                e = ends[0:EP, n, :]
                v.tensor_scalar(tmpi[0:EP, :], e, 7, None, ALU.logical_shift_right)
                link(v.tensor_scalar(sloti[0:EP, :], e, P - 1, None, ALU.bitwise_and))
                v.tensor_copy(tilef[0:EP, :], tmpi[0:EP, :])
                link(v.tensor_copy(rowf[0:EP, :], sloti[0:EP, :]))
                v.tensor_tensor(th, tilef[0:EP, None, :].broadcast_to([EP, NJ, ET]),
                                iota_j[0:EP, :, None].broadcast_to([EP, NJ, ET]), ALU.is_equal)
                v.tensor_tensor(rh, rowf[0:EP, :, None].broadcast_to([EP, ET, P]),
                                iota_p[0:EP, None, :].broadcast_to([EP, ET, P]), ALU.is_equal).then_inc(q_hot, 1)

            def exponent(dst_, src_, lo, hi):
                link(v.tensor_scalar(dst_, src_.bitcast(INT32), 23, None, ALU.logical_shift_right))
                link(v.tensor_scalar(dst_, dst_, lo, hi, ALU.max, ALU.min))

            def power(dst_, tmp, exp, mul, add):
                link(v.tensor_scalar(tmp, exp, mul, add, ALU.mult, ALU.add))
                link(v.tensor_scalar(dst_.bitcast(INT32), tmp, 23, None, ALU.logical_shift_left))

            one_hots(0)
            dve.wait_ge(q_deg, 1)
            v.tensor_scalar(dis[:, :], p_self[0][:, 0:NJ], 1.0, None, ALU.add).then_inc(q_sqin, 1)
            one_hots(1)
            dve.wait_ge(q_hot, 2)
            link(v.tensor_tensor_scan(before[0:EP, :], notfirst[0:EP, :], tile_hot[0:EP, :], 0.0, ALU.mult, ALU.add))
            bt = before[0:EP, :].rearrange("p (j t) -> p j t", t=ET)
            st = summed[0:EP, :].rearrange("p (j t) -> p j t", t=ET)
            v.tensor_copy(rowtot[0:EP, :], bt[:, :, ET - 1]).then_inc(q_rowtot, 1)
            dve.wait_ge(q_base, 1)
            link(v.tensor_scalar(ki[:, :], p_out[1][:, 0:NJ], float(P - 1), None, ALU.add))
            link(v.tensor_scalar(ki[:, :], ki[:, :], 7, None, ALU.logical_shift_right))
            link(v.tensor_scalar(kf[:, :], ki[:, :], 1.0, None, ALU.max))
            link(v.tensor_tensor_scan(cincl[:, :], ones_j[:, :], kf[:, :], 0.0, ALU.mult, ALU.add))
            link(v.tensor_tensor(cexcl[:, :], cincl[:, :], kf[:, :], ALU.subtract))
            link(v.tensor_copy(cfirst[0:1, :], cexcl[0:1, :]))
            v.memset(cfirst[0:1, NT:NT + 1], NC).then_inc(q_cf, 1)
            link(v.tensor_scalar(cexcl[:, :], cexcl[:, :], float(P), -1.0, ALU.mult, ALU.add))
            link(v.tensor_tensor(cbase[0:EP, :], cexcl[0:EP, :], p_out[0][0:EP, 0:NJ], ALU.add))
            link(v.tensor_tensor(st, bt, cbase[0:EP, :, None].broadcast_to([EP, NJ, ET]), ALU.add))
            link(v.tensor_tensor(st, st, th, ALU.mult))
            link(v.tensor_reduce(slotf[0:EP, :], summed[0:EP, :].rearrange("p (j t) -> p t j", t=ET), AX_X, ALU.add))
            link(v.tensor_copy(sloti[0:EP, :], slotf[0:EP, :]))
            v.tensor_scalar(slotp[0:EP, :], sloti[0:EP, :], P - 1, None, ALU.bitwise_and)
            link(v.tensor_scalar(slotc[0:EP, :], sloti[0:EP, :], 7, None, ALU.logical_shift_right))
            v.scalar_tensor_tensor(slotrow[0:EP, :], slotp[0:EP, :], float(NC), slotc[0:EP, :], ALU.mult, ALU.add)
            v.tensor_copy(rec[0:EP, :, 0], ends[0:EP, 0, :])
            v.memset(rec[0:EP, :, 3], 0)
            link(v.tensor_scalar(rec[0:EP, :, 2], ends[0:EP, 1, :], P - 1, None, ALU.bitwise_and))
            dve.sem_inc(q_slot, 1)
            dve.wait_ge(q_deg, 2)
            v.tensor_copy(deg[:, :], p_self[1][:, 0:NJ])
            link(v.tensor_scalar(indeg1[:, :], p_self[1][:, 0:NJ], 1.0, None, ALU.add))
            dve.sem_inc(q_degsb, 1)
            v.tensor_scalar(has[:, :], deg[:, :], 1.0, None, ALU.min)
            link(v.tensor_scalar(rdeg[:, :], deg[:, :], 1.0, None, ALU.max))
            dve.wait_ge(q_sq, 1)
            v.reciprocal(dis[:, :], sqd[:, :])
            link(v.reciprocal(rdeg[:, :], rdeg[:, :]))
            link(v.tensor_scalar(dis1k[:, :], dis[:, :], ASCALE, None, ALU.mult))
            link(v.tensor_copy(dishl[:, :, 0], dis1k[:, :]))
            link(v.tensor_tensor(dishl[:, :, 1], dis1k[:, :], dishl[:, :, 0], ALU.subtract))
            for n in range(6):
                dve.wait_ge(q_w[n % 2], 16 * (n // 2 + 1))
                v.tensor_reduce(wmax[:, n:n + 1], wst[n % 2], AX_X, ALU.max,
                                apply_absolute_value=True).then_inc(q_wmax, 1)
                dve.wait_ge(q_wmaxall, n + 1)
                exponent(wexp[:, 0:1], wmaxall[:, n:n + 1], 30, 240)
                power(wscale[:, n:n + 1], wexp[:, 1:2], wexp[:, 0:1], -1.0, 268.0)
                power(unscale[:, n:n + 1], wexp[:, 2:3], wexp[:, 0:1], 1.0, -24.0)
                dve.sem_inc(q_wsc, 1)
                for k in range(KD):
                    m = KD * n + k
                    dve.wait_ge(q_whi, m + 1)
                    v.scalar_tensor_tensor(wlo[NAMES[n]][:, k, :], p_agg[m % 2][:, :], wscale[:, n:n + 1],
                                           whi[NAMES[n]][:, k, :], ALU.mult, ALU.subtract).then_inc(q_wlo, 1)
            dve.wait_ge(q_degmax, 1)
            exponent(dexp[:, :], degmax[:, :], 1, 250)
            power(down[:, :], ki[:, :], dexp[:, :], -1.0, 253.0)
            power(up[:, :], ki[:, :], dexp[:, :], 1.0, 1.0)
            link(v.tensor_scalar(rt[1][:, :], rdeg[:, :], 1 / ASCALE, None, ALU.mult))
            link(v.scalar_tensor_tensor(rt[0][:, :], up[:, :], UN["W0"], dis[:, :], ALU.mult, ALU.mult))
            link(v.scalar_tensor_tensor(rt[2][:, :], up[:, :], UN["Wl"], rdeg[:, :], ALU.mult, ALU.mult))
            link(v.scalar_tensor_tensor(rt[3][:, :], up[:, :], UN["Wneigh"], rdeg[:, :], ALU.mult, ALU.mult))

            class Steps:
                def __init__(self, base, per):
                    self.base, self.per, self.k = base, per, 0

                def start(self, t):
                    self.t, self.k = t, 0

                def link(self, ins):
                    self.k += 1
                    ins.then_inc(step, 1)
                    dve.wait_ge(step, self.t * self.per + (self.base + self.k))

                def end(self):
                    assert self.k == self.per, (self.k, self.per)

            def moments(st_, data, out_):
                st_.link(v.bn_stats(stats[:, :], data))
                apart(dve)
                return v.bn_aggr(out_, stats[:, :])

            def scales(ph, t, s, st_):
                dve.wait_ge(std1, NT * ph + t + 1)
                col = bass.ds(t, 1)
                if ph == 0:
                    st_.link(v.reciprocal(rtmp[:, :], std[s][:, :]))
                    st_.link(v.tensor_tensor(rstd[:, col], rtmp[:, :], dis[:, col], ALU.mult))
                else:
                    st_.link(v.reciprocal(rstd[:, col], std[s][:, :]))
                v.scalar_tensor_tensor(nbias[:, col], mv[s][:, 0:1], -1.0, rstd[:, col], ALU.mult,
                                       ALU.mult).then_inc(scale1, 1)

            def low(ph, t, s):
                dve.wait_ge(hi_ready, NT * ph + t + 1)
                if ph == 0:
                    v.tensor_copy(hout[s][:, 2 * D:2 * D + 2], dishl[:, bass.ds(t, 1), :])
                v.tensor_tensor(hout[s][:, D:2 * D], h32[s][:, :], hout[s][:, 0:D], ALU.subtract).then_inc(lo_ready, 1)

            steps = Steps(0, 3)

            def phase0(t, s, last):
                steps.start(t)
                dve.wait_ge(x_loaded[s], 16 * (in_slot(0, t, s) + 1))
                moments(steps, xbuf[s][:, :], mv[s][:, :]).then_inc(var1, 1)
                scales(0, t, s, steps)
                low(0, t, s)
                dve.sem_inc(x_used, 1)
                steps.end()
            tiles(dve, phase0)

            dve.wait_ge(q_rec, 16)
            link(v.tensor_copy(relf[:, :], recback[:, 0:NC, 2]))
            link(v.tensor_tensor(select[:, :].rearrange("p (c r) -> p c r", r=P),
                                 relf[:, :, None].broadcast_to([P, NC, P]),
                                 iota_p[:, None, :].broadcast_to([P, NC, P]), ALU.is_equal))
            dve.sem_inc(q_sel, 1)
            dve.sem_inc(q_ready, 1)

            base = 3 * NT
            for L in range(4):
                ph = L + 1
                per = [5, 11, 5, 7][L]
                st_ = Steps(base, per)
                base += per * NT
                col = lambda t: bass.ds(t, 1)

                def evacuate(t, s):
                    if L != 1:
                        dve.wait_ge(agg_hi, NT * L + t + 3)
                        v.scalar_tensor_tensor(aggh[s][:, D:2 * D], p_agg[s][:, :], down[:, col(t)],
                                               aggh[s][:, 0:D], ALU.mult, ALU.subtract).then_inc(agg_lo, 1)

                def epilogue(t, s, last):
                    st_.start(t)
                    rs = rt[L][:, col(t)]
                    if L == 0:
                        dve.wait_ge(agg_ps, t + 1)
                        st_.link(v.scalar_tensor_tensor(s1[:, :], p_norm[:, 8 * s:8 * s + 1], 1 / ASCALE,
                                                        dis[:, col(t)], ALU.mult, ALU.add))
                        v.tensor_tensor(s2[s][:, :], s1[:, :], dis[:, col(t)], ALU.mult).then_inc(norm_in, 1)
                        dve.wait_ge(out_ps, t + 1)
                        dve.wait_ge(brow, t + 1)
                        st_.link(v.scalar_tensor_tensor(ubuf[s], p_out[s][:, :], rs, tbuf, ALU.mult, ALU.add))
                    else:
                        dve.wait_ge(out_ps, NT * L + t + 1)
                        bias = rows[[None, "bu", "bl", "bias3"][L]][:, :]
                        un = UN[[None, "Wu1", "Wr", "Wself"][L]]
                        st_.link(v.scalar_tensor_tensor(tbuf, p_self[s][:, :], un, bias, ALU.mult, ALU.add))
                        if L == 1:
                            st_.link(v.scalar_tensor_tensor(t2buf, rows["vb"][:, :], has[:, col(t)], tbuf,
                                                            ALU.mult, ALU.add))
                        st_.link(v.scalar_tensor_tensor(ubuf[s], p_out[s][:, :], rs, t2buf if L == 1 else tbuf,
                                                        ALU.mult, ALU.add))
                    dve.sem_inc(mixed, 1)
                    dve.wait_ge(x_loaded[s], 16 * (in_slot(ph, t, s) + 1))
                    wait_stored(ph, t, s)
                    if L in (0, 2):
                        st_.link(v.scalar_tensor_tensor(xnew[s][:, :], ubuf[s], 0.0, xbuf[s][:, :], ALU.max, ALU.add))
                    else:
                        if L == 1:
                            dve.sem_inc(u_ready, 1)
                            dve.wait_ge(g_ready, t + 1)
                            st_.link(v.scalar_tensor_tensor(t2buf, habuf[:, :], 1 / ASCALE, gbuf[:, :],
                                                            ALU.mult, ALU.add))
                            dve.sem_inc(g_used, 1)
                            y, gam, bet = t2buf, "g1", "be1"
                        else:
                            y, gam, bet = ubuf[s], "g3", "be3"
                        moments(st_, y, mv2[:, :]).then_inc(var2, 1)
                        dve.wait_ge(std2_ready, NT * (L // 2) + t + 1)
                        st_.link(v.reciprocal(rstd2[:, :], std2[:, :]))
                        st_.link(v.scalar_tensor_tensor(tbuf, y, mv2[:, 0:1], rows[gam][:, :], ALU.subtract, ALU.mult))
                        st_.link(v.scalar_tensor_tensor(tbuf, tbuf, rstd2[:, :], xbuf[s][:, :], ALU.mult, ALU.add))
                        st_.link(v.tensor_tensor(xnew[s][:, :], tbuf, rows[bet][:, :], ALU.add))
                    dve.sem_inc(x_used, 1)
                    if L < 3:
                        moments(st_, xnew[s][:, :], mv[s][:, :]).then_inc(var1, 1)
                        scales(ph, t, s, st_)
                        low(ph, t, s)
                    else:
                        dve.sem_inc(var1, 1)
                    st_.end()

                def wait_stored(ph, t, s):
                    per_ = (NT + 1) // 2 if s == 0 else NT // 2
                    dve.wait_ge(stored[s], 16 * (per_ + (ph - 1) * 2 * per_ + (1 if ph == 4 else 2) * half(t, s)))

                evacuate(0, 0)
                with dve.Fori(0, PAIRS) as i:
                    evacuate(2 * i + 1, 1)
                    epilogue(2 * i, 0, False)
                    evacuate(2 * i + 2, 0)
                    epilogue(2 * i + 1, 1, False)
                epilogue(NT - 1, 0, True)


_INS = ["x", "src", "dst", "edge_attr_512", "L0_gnn_W", "L0_gnn_b", "L1_gnn_Wm", "L1_gnn_bm", "L1_gnn_Wu", "L1_gnn_bu",
        "L1_gnn_gamma", "L1_gnn_beta", "L2_gnn_W_l", "L2_gnn_b_l", "L2_gnn_W_r", "L3_gnn_W_self", "L3_gnn_W_neigh",
        "L3_gnn_bias", "L3_gnn_gamma", "L3_gnn_beta"]


def kernel(**inputs):
    import concourse.bacc as bacc
    from concourse.bass_utils import run_bass_kernel_spmd as run

    nc = bacc.Bacc("TRN2", target_bir_lowering=False, num_devices=1)
    arrays, args = {}, []
    for name in _INS:
        a = np.ascontiguousarray(inputs[name])
        arrays[f"in_{name}"] = a
        args.append(nc.dram_tensor(f"in_{name}", a.shape, mybir.dt.from_np(a.dtype), kind="ExternalInput").ap())
    o = nc.dram_tensor("out_x", (N, D), FP32, kind="ExternalOutput").ap()
    gnn_kernel(nc, *args, o)
    r = run(nc, [arrays], core_ids=[0])
    return r.results[0]["out_x"]
```
